# Optimizing a Trainium2 kernel written in Bass

```python
import numpy as np
import jax
import jax.numpy as jnp

def _softmax(x, axis=-1):
    return jax.nn.softmax(x, axis=axis)

def _gelu(x):
    return jax.nn.gelu(x, approximate=True)

def _silu(x):
    return jax.nn.silu(x)

def _sigmoid(x):
    return jax.nn.sigmoid(x)

def _layernorm(x, axis=-1, eps=1e-05):
    m = jnp.mean(x, axis=axis, keepdims=True)
    v = jnp.var(x, axis=axis, keepdims=True)
    return (x - m) / jnp.sqrt(v + eps)

def _scatter_add(tgt, idx, src, axis=0):
    return tgt.at[idx].add(src)

def _segment_sum(src, seg, n):
    return jax.ops.segment_sum(src, seg, n)
kernel_name = 'mk_adj_resnorm_d2_adj_r2_3642c5'

def setup_inputs(seed: int=0):
    np.random.seed(seed)
    _w = jnp.asarray

    def _rec_inputs():
        import jax
        import jax.numpy as jnp
        _gk = jax.random.key(seed)
        x = 7.22e-05 + 1 * jax.random.normal(jax.random.fold_in(_gk, 1), (4096, 512), jnp.float32)
        _a = jax.random.bernoulli(jax.random.fold_in(_gk, 2), 0.000488281, (4096, 4096))
        _a = jnp.logical_or(_a, jnp.swapaxes(_a, -1, -2))
        _a = jnp.logical_or(_a, jnp.eye(4096, dtype=bool))
        _af = _a.astype(jnp.float32)
        _af = _af * jax.random.uniform(jax.random.fold_in(_gk, 3), (4096, 4096), jnp.float32, 0.05, 1)
        adj = _af
        return (x, adj)
    x, adj = _rec_inputs()

    def _L0_gnn_setup():
        import jax, jax.numpy as jnp
        import numpy as np
        N = 4096
        IN_FEATURES = 512
        OUT_FEATURES = 512
        key = jax.random.key(seed)
        k_x, k_adj, k_w, k_b = jax.random.split(key, 4)
        x = jax.random.normal(k_x, (N, IN_FEATURES), dtype=jnp.float32)
        adj = jax.random.uniform(k_adj, (N, N), dtype=jnp.float32)
        stdv = 1.0 / np.sqrt(OUT_FEATURES)
        weight = jax.random.uniform(k_w, (IN_FEATURES, OUT_FEATURES), dtype=jnp.float32, minval=-stdv, maxval=stdv)
        bias = jax.random.uniform(k_b, (OUT_FEATURES,), dtype=jnp.float32, minval=-stdv, maxval=stdv)
        return {'x': x, 'adj': adj, 'weight': weight, 'bias': bias}
    _L0_gnn_all = _L0_gnn_setup()
    _L0_gnn_in = {k: v for k, v in _L0_gnn_all.items() if k in ('weight', 'bias')}
    del _L0_gnn_all

    def _L1_gnn_setup():
        import jax, jax.numpy as jnp
        import numpy as np
        ALPHA = 0.2
        NEG = -9000000000000000.0
        N, NFEAT, NHID, NHEADS = (2048, 512, 64, 8)
        EMB = NHID * NHEADS
        key = jax.random.key(seed)
        ks = jax.random.split(key, 16)
        x = jax.random.normal(ks[0], (N, NFEAT), dtype=jnp.float32)
        adj = (jax.random.uniform(ks[1], (N, N)) < 0.01).astype(jnp.float32)
        adj = jnp.maximum(adj, jnp.eye(N, dtype=jnp.float32))
        s = 0.05
        W = jax.random.normal(ks[2], (NHEADS, NFEAT, NHID), dtype=jnp.float32) * s
        a1 = jax.random.normal(ks[3], (NHEADS, NHID), dtype=jnp.float32) * s
        a2 = jax.random.normal(ks[4], (NHEADS, NHID), dtype=jnp.float32) * s
        W1 = jax.random.normal(ks[5], (EMB // 2, EMB), dtype=jnp.float32) * s
        b1 = jnp.zeros((EMB // 2,), dtype=jnp.float32)
        W2 = jax.random.normal(ks[6], (NFEAT // 4, EMB // 2), dtype=jnp.float32) * s
        b2 = jnp.zeros((NFEAT // 4,), dtype=jnp.float32)
        W3 = jax.random.normal(ks[7], (NFEAT // 2, NFEAT // 4), dtype=jnp.float32) * s
        b3 = jnp.zeros((NFEAT // 2,), dtype=jnp.float32)
        W4 = jax.random.normal(ks[8], (NFEAT, NFEAT // 2), dtype=jnp.float32) * s
        b4 = jnp.zeros((NFEAT,), dtype=jnp.float32)
        return {'x': x, 'adj': adj, 'W': W, 'a1': a1, 'a2': a2, 'W1': W1, 'b1': b1, 'W2': W2, 'b2': b2, 'W3': W3, 'b3': b3, 'W4': W4, 'b4': b4}
    _L1_gnn_all = _L1_gnn_setup()
    _L1_gnn_in = {k: v for k, v in _L1_gnn_all.items() if k in ('W', 'a1', 'a2', 'W1', 'b1', 'W2', 'b2', 'W3', 'b3', 'W4', 'b4')}
    del _L1_gnn_all
    return {'x': x, 'adj': adj, 'L0_gnn_weight': _L0_gnn_in['weight'], 'L0_gnn_bias': _L0_gnn_in['bias'], 'L1_gnn_W': _L1_gnn_in['W'], 'L1_gnn_a1': _L1_gnn_in['a1'], 'L1_gnn_a2': _L1_gnn_in['a2'], 'L1_gnn_W1': _L1_gnn_in['W1'], 'L1_gnn_b1': _L1_gnn_in['b1'], 'L1_gnn_W2': _L1_gnn_in['W2'], 'L1_gnn_b2': _L1_gnn_in['b2'], 'L1_gnn_W3': _L1_gnn_in['W3'], 'L1_gnn_b3': _L1_gnn_in['b3'], 'L1_gnn_W4': _L1_gnn_in['W4'], 'L1_gnn_b4': _L1_gnn_in['b4']}

def reference(x, adj, L0_gnn_weight, L0_gnn_bias, L1_gnn_W, L1_gnn_a1, L1_gnn_a2, L1_gnn_W1, L1_gnn_b1, L1_gnn_W2, L1_gnn_b2, L1_gnn_W3, L1_gnn_b3, L1_gnn_W4, L1_gnn_b4):
    import jax
    import jax.numpy as jnp

    def _L0_gnn_ref(x, adj, weight, bias):
        import jax, jax.numpy as jnp
        import numpy as np
        N = 4096
        IN_FEATURES = 512
        OUT_FEATURES = 512
        support = jnp.matmul(x, weight)
        output = jnp.matmul(adj, support)
        return output + bias

    def _L1_gnn_ref(x, adj, W, a1, a2, W1, b1, W2, b2, W3, b3, W4, b4):
        import jax, jax.numpy as jnp
        import numpy as np
        ALPHA = 0.2
        NEG = -9000000000000000.0
        N, NFEAT, NHID, NHEADS = (2048, 512, 64, 8)
        EMB = NHID * NHEADS
        Wh = jnp.einsum('nf,hfd->hnd', x, W)
        e_src = jnp.einsum('hnd,hd->hn', Wh, a1)
        e_dst = jnp.einsum('hnd,hd->hn', Wh, a2)
        e = jax.nn.leaky_relu(e_src[:, :, None] + e_dst[:, None, :], ALPHA)
        e = jnp.where(adj[None] > 0, e, NEG)
        att = jax.nn.softmax(e, axis=-1)
        h = jnp.einsum('hnm,hmd->hnd', att, Wh)
        h = jax.nn.elu(h)
        enc = jnp.transpose(h, (1, 0, 2)).reshape(x.shape[0], -1)
        out = jax.nn.relu(enc @ W1.T + b1)
        out = jax.nn.relu(out @ W2.T + b2)
        out = jax.nn.relu(out @ W3.T + b3)
        out = out @ W4.T + b4
        return out
    x = _layernorm(x + _L0_gnn_ref(x, adj, L0_gnn_weight, L0_gnn_bias), axis=-1)
    x = _layernorm(x + _L1_gnn_ref(x, adj, L1_gnn_W, L1_gnn_a1, L1_gnn_a2, L1_gnn_W1, L1_gnn_b1, L1_gnn_W2, L1_gnn_b2, L1_gnn_W3, L1_gnn_b3, L1_gnn_W4, L1_gnn_b4), axis=-1)
    return x

_drawn_inputs = setup_inputs


def setup_inputs(seed=0):
    import zlib

    import numpy as np

    out = dict(_drawn_inputs(seed))
    spreads = {'L1_gnn_b1': (0.0, 0.674),
     'L1_gnn_b2': (0.0, 0.345),
     'L1_gnn_b3': (0.0, 0.1),
     'L1_gnn_b4': (0.0, 0.1)}
    factors = {'L0_gnn_bias': 2.906, 'L1_gnn_a1': 23.79, 'L1_gnn_a2': 3.73}
    for name, (base, spread) in spreads.items():
        noise = np.random.default_rng([zlib.crc32(name.encode()), seed]).standard_normal(out[name].shape)
        drawn = base * np.exp(spread * noise) if base else spread * noise
        out[name] = jnp.asarray(drawn.astype(out[name].dtype))
    for name, factor in factors.items():
        out[name] = (out[name] * factor).astype(out[name].dtype)
    return out
```

```python
import numpy as np
import concourse.bass as bass
from concourse import mybir
from contextlib import ExitStack

F32 = mybir.dt.float32
U32 = mybir.dt.uint32
ALU = mybir.AluOpType
ACT = mybir.ActivationFunctionType
AX = mybir.AxisListType

P = 128
N = 4096
F = 512
HEADS, HID = 8, 64
T = N // P
FC = F // P
K = 16
R8 = 8
ROW = F + 2 * HEADS
GROUP = 4
NG = T // GROUP
M1, M2, M3 = 256, 128, 256
EPS = 1e-5
ALPHA = 0.2
LOWEST = -3.0e38
STEPS = N // K
GEN = 16
NEG = 9.0e15
FIND, NORM, ATT = 8, 3, 8
SKIP = 65536.0
CREDIT = 2


class Chain:

    def __init__(self, eng, sem, base=0):
        self.eng, self.sem, self.base, self.n = eng, sem, base, 0

    def step(self, ins):
        self.n += 1
        ins.then_inc(self.sem, 1)

    def wait(self):
        self.eng.wait_ge(self.sem, self.base + self.n)

    def link(self, ins):
        self.step(ins)
        self.wait()


def build(nc, d):
    ctx = ExitStack()
    with ctx:
        def sb(name, shape, dt=F32):
            return ctx.enter_context(nc.sbuf_tensor(name, shape, dt))

        def ps(name, shape):
            return ctx.enter_context(nc.psum_tensor(name, shape, F32))

        def sem(name):
            return ctx.enter_context(nc.semaphore(name))

        arena = sb("arena", [P, T * F + 2 * N])
        support = arena[:, 0:T * F].rearrange("p (t f) -> p t f", f=F)
        strip = [arena[:, T * F + b * N:T * F + (b + 1) * N].rearrange("p (c i) -> p c i", i=P) for b in range(2)]
        gath = [arena[:, b * K * ROW:(b + 1) * K * ROW].rearrange("p (k r) -> p k r", r=ROW) for b in range(2)]
        nat2 = sb("nat2", [P, 2, N])
        nat = [nat2[:, b, :] for b in range(2)]
        rest = sb("rest", [P, N])
        w0 = sb("w0", [P, FC, F])
        wcat = sb("wcat", [P, FC, F])
        a12 = sb("a12", [P, 2, F])
        bias0 = sb("bias0", [P, F])
        w1 = sb("w1", [P, FC, M1])
        w2 = sb("w2", [P, M1 // P, M2])
        w3 = sb("w3", [P, M2 // P, M3])
        w4 = sb("w4", [P, M3 // P, F])
        b1 = sb("b1", [P, M1 // P])
        b2 = sb("b2", [P, M2 // P])
        b3 = sb("b3", [P, M3 // P])
        b4 = sb("b4", [1, F])
        ones = sb("ones", [1, P])
        onesc = sb("onesc", [P, 1])
        ident = sb("ident", [P, P])
        eps = sb("eps", [P, 1])
        minus1 = sb("minus1", [P, 1])
        xT = rest[:, 0:2 * F].rearrange("p (b c i) -> p b c i", b=2, i=P)
        xn = sb("xn", [P, 2, F])
        x1 = sb("x1", [P, 2, F])
        x1T = sb("x1T", [P, FC, P])
        row = sb("row", [P, 2, ROW])
        prod = sb("prod", [P, 2, F])
        stats = sb("stats", [P, 6])
        mv = sb("mv", [P, 2])
        sd = sb("sd", [P, 1])
        rstd = sb("rstd", [P, 1])
        top = sb("top", [P, K])
        topi = sb("topi", [P, K], U32)
        off = sb("off", [P, K])
        cap = sb("cap", [P, T * K])
        nbr = sb("nbr", [P, T * K], U32)
        late = nat2[:, :, :].rearrange("p b n -> p (b n)")
        encT = late[:, 0:FC * GROUP * P].rearrange("p (c i) -> p c i", c=FC)
        h1 = late[:, 2048:3072].rearrange("p (c i) -> p c i", c=M1 // P)
        h3 = late[:, 3072:4096].rearrange("p (c i) -> p c i", c=M3 // P)
        h2 = late[:, 4096:4608]
        y = late[:, 4608:4608 + GROUP * F].rearrange("p (j f) -> p j f", f=F)
        x1r = rest[:, 0:GROUP * F].rearrange("p (j f) -> p j f", f=F)
        en = rest[:, 2048:2560]
        hneg = rest[:, 2560:3072]
        hexp = rest[:, 3072:3584]
        idx = sb("idx", [P, 2, K], U32)
        e_src = sb("e_src", [P, T * HEADS])
        z = sb("z", [P, K, HEADS])
        e = sb("e", [P, K, HEADS])
        zmax = sb("zmax", [P, HEADS])
        zsum = sb("zsum", [P, HEADS])
        zrec = sb("zrec", [P, HEADS])
        stats2 = sb("stats2", [P, 6])
        mv2 = sb("mv2", [P, GROUP, 2])
        sd2 = sb("sd2", [P, GROUP])
        rstd2 = sb("rstd2", [P, GROUP])
        flagp = sb("flagp", [P, 2])
        flag = sb("flag", [1, 1], U32)
        gen_rows = arena[:, 0:K * ROW]
        gen_g = gath[0]
        gen_adj = arena[:, K * ROW:K * ROW + N]
        gen_h, gen_part = prod[:, 0, :], prod[:, 1, :]
        gen_cap = top
        gen_m = sb("gen_m", [P, HEADS])
        gen_scale = sb("gen_scale", [P, HEADS])
        gen_fade = sb("gen_fade", [P, HEADS])

        bank = [ps(f"bank{i}", [P, F]) for i in range(8)]
        acc = bank[0:2]
        trp = bank[2]
        whp = bank[3]
        mlp = [bank[4], bank[5]]
        outp = [bank[6], bank[7]]

        consts_in = sem("consts_in")
        waits_alone = sem("waits_alone")
        consts_set = sem("consts_set")
        ident_zero = sem("ident_zero")
        xT_in = [sem(f"xT_in{b}") for b in range(2)]
        support_mm = sem("support_mm")
        support_act = sem("support_act")
        support_dve = sem("support_dve")
        strip_in = [sem(f"strip_in{b}") for b in range(2)]
        nat_in = [sem(f"nat_in{b}") for b in range(2)]
        xn_in = [sem(f"xn_in{b}") for b in range(2)]
        layer0_mm = sem("layer0_mm")
        nat_used = sem("nat_used")
        xb_ready = sem("xb_ready")
        var_ready = sem("var_ready")
        sd_ready = sem("sd_ready")
        x1_ready = sem("x1_ready")
        x1_stored = [sem(f"x1_stored{b}") for b in range(2)]
        x1T_tr = sem("x1T_tr")
        x1T_ready = sem("x1T_ready")
        wh_mm = sem("wh_mm")
        wh_ready = sem("wh_ready")
        row_ready = sem("row_ready")
        src_kept = sem("src_kept")
        row_stored = [sem(f"row_stored{b}") for b in range(2)]
        dve_find = sem("dve_find")
        dve_norm = sem("dve_norm")
        dve_row = sem("dve_row")
        idx_ready = sem("idx_ready")
        gathered = [sem(f"gathered{b}") for b in range(2)]
        x1r_in = sem("x1r_in")
        z_ready = sem("z_ready")
        e_ready = sem("e_ready")
        weighted = sem("weighted")
        sum_mm = sem("sum_mm")
        hneg_ready = sem("hneg_ready")
        hexp_ready = sem("hexp_ready")
        en_ready = sem("en_ready")
        en_tr = sem("en_tr")
        encT_ready = sem("encT_ready")
        mlp_mm = sem("mlp_mm")
        mlp_act = sem("mlp_act")
        out_mm = sem("out_mm")
        y_copied = sem("y_copied")
        var2_ready = sem("var2_ready")
        sd2_ready = sem("sd2_ready")
        y_ready = sem("y_ready")
        out_stored = sem("out_stored")
        dve_att = sem("dve_att")
        dve_en = sem("dve_en")
        dve_ln2 = sem("dve_ln2")
        flagp_ready = sem("flagp_ready")
        flag_mm = sem("flag_mm")
        flag_ready = sem("flag_ready")
        gen_adj_in = sem("gen_adj_in")
        gen_rows_in = sem("gen_rows_in")
        gen_rows_used = sem("gen_rows_used")
        gen_z = sem("gen_z")
        gen_e = sem("gen_e")
        gen_h_ready = sem("gen_h_ready")
        dve_gen = sem("dve_gen")

        CONSTS = [(w0, "w0"), (wcat, "wcat"), (w1, "w1"), (w2, "w2"), (w3, "w3"), (w4, "w4"),
                  (b1, "b1"), (b2, "b2"), (b3, "b3")]

        x_t = d["x"].rearrange("(t p) f -> t p f", p=P)
        adj_t = d["adj"].rearrange("(t p) n -> t p n", p=P)
        x1_t = d["x1"].rearrange("(t p) f -> t p f", p=P)
        x1_g = d["x1"].rearrange("(g j p) f -> g p j f", p=P, j=GROUP)
        out_g = d["out"].rearrange("(g j p) f -> g p j f", p=P, j=GROUP)
        table_t = d["table"].rearrange("(t p) r -> t p r", p=P)

        def alone(eng):
            eng.sem_inc(waits_alone, 1)

        table_k = d["table"].rearrange("(s k) r -> s (k r)", k=K)

        block = ctx.enter_context(nc.Block())

        @block.sync
        def _(sp):
            for b in range(2):
                sp.sem_inc(x1_stored[b], 16)
                sp.sem_inc(row_stored[b], 16)
            for tile, name in CONSTS:
                sp.dma_start(tile[:], d[name]).then_inc(consts_in, 16)
            sp.dma_start(a12[:].rearrange("p a f -> p (a f)"), d["a12"].to_broadcast([P, 2 * F])).then_inc(consts_in, 16)
            sp.dma_start(bias0[:], d["bias0"].to_broadcast([P, F])).then_inc(consts_in, 16)
            sp.dma_start(b4[:], d["b4"]).then_inc(consts_in, 16)
            with sp.Fori(0, T // 2) as n:
                for b in range(2):
                    t = n * 2 + b
                    sp.wait_ge(support_mm, t + 1)
                    sp.dma_start(xT[:, b, :, :], d["xT"][t]).then_inc(xT_in[b], 16)
            def loads(n, b):
                t = n * 2 + b
                sp.wait_ge(layer0_mm, t + 1)
                sp.dma_start(strip[b], d["adjT"][t]).then_inc(strip_in[b], 16)
                sp.wait_ge(nat_used, t + 1)
                sp.dma_start(nat[b], adj_t[t]).then_inc(nat_in[b], 16)
                sp.wait_ge(x1_ready, t + 1)
                sp.dma_start(xn[:, b, :], x_t[t]).then_inc(xn_in[b], 16)

            def stores(n, b):
                t = n * 2 + b
                sp.wait_ge(x1_ready, t + 1 + CREDIT)
                sp.dma_start(x1_t[t], x1[:, b, :]).then_inc(x1_stored[b], 16)
                sp.wait_ge(row_ready, t + 1)
                sp.dma_start(table_t[t], row[:, b, :]).then_inc(row_stored[b], 16)

            for b in range(2):
                loads(0, b)
            with sp.Fori(1, T // 2) as n:
                for b in range(2):
                    loads(n, b)
                    stores(n - 1, b)
            for b in range(2):
                stores(T // 2 - 1, b)
            for b in range(2):
                sp.wait_ge(row_stored[b], 16 * (T // 2 + 1))
                sp.wait_ge(x1_stored[b], 16 * (T // 2 + 1))

            def store(g):
                sp.wait_ge(y_ready, g + 1)
                sp.dma_start(out_g[g], y).then_inc(out_stored, 16)

            def load_x1(g):
                sp.dma_start(x1r, x1_g[g]).then_inc(x1r_in, 16)

            sp.wait_ge(dve_find, FIND * T)
            load_x1(0)
            with sp.Fori(1, NG) as g:
                store(g - 1)
                load_x1(g)
            store(NG - 1)
            sp.wait_ge(out_stored, 16 * NG)
            sp.wait_ge(flag_ready, 1)
            with sp.If(sp.value_load(flag[0:1, 0:1]) > 0):
                with sp.Fori(NG, 2 * NG) as g:
                    sp.wait_ge(y_ready, g)
                    sp.dma_start(x1r, x1_g[g - NG]).then_inc(x1r_in, 16)
                    with sp.Fori(0, GROUP) as j:
                        t = (g - NG) * GROUP + j
                        sp.wait_ge(gen_rows_used, t * STEPS + 1)
                        sp.dma_start(gen_adj, adj_t[t]).then_inc(gen_adj_in, 16)
                        with sp.Fori(0, STEPS) as k:
                            sp.wait_ge(gen_rows_used, t * STEPS + k + 1)
                            sp.dma_start(gen_rows, table_k[bass.ds(k, 1), :].to_broadcast([P, K * ROW])).then_inc(gen_rows_in, 16)
                    sp.wait_ge(y_ready, g + 1)
                    sp.dma_start(out_g[g - NG], y).then_inc(out_stored, 16)
                sp.wait_ge(out_stored, 16 * 2 * NG)

        @block.vector
        def _(dve):
            dve.sem_inc(nat_used, CREDIT)
            dve.sem_inc(gen_rows_used, 1)
            dve.sem_inc(src_kept, CREDIT)
            dve.sem_inc(x1_ready, CREDIT)
            dve.sem_inc(en_ready, CREDIT)
            dve.sem_inc(support_dve, 1)
            nc.vector.memset(ones[:], 1.0).then_inc(consts_set, 1)
            nc.vector.memset(onesc[:], 1.0).then_inc(consts_set, 1)
            nc.vector.memset(eps[:], EPS).then_inc(consts_set, 1)
            nc.vector.memset(minus1[:], -1.0).then_inc(consts_set, 1)
            with dve.Fori(0, T // 2) as n:
                dve.wait_ge(support_mm, n * 2 + 2 + CREDIT)
                nc.vector.tensor_copy(support[:, n * 2 + 1, :], acc[1][:]).then_inc(support_dve, 1)

            def find(n, b):
                t = n * 2 + b
                c = Chain(dve, dve_find, t * FIND)
                dve.wait_ge(nat_in[b], 16 * (n + 1))
                alone(dve)
                c.step(nc.vector.max(top[:, 0:R8], nat[b]))
                c.wait()
                alone(dve)
                nc.vector.max_index(topi[:, 0:R8], top[:, 0:R8], nat[b]).then_inc(dve_find, 1)
                c.n += 1
                nc.vector.match_replace(rest[:], top[:, 0:R8], nat[b], -1.0).then_inc(nat_used, 1)
                dve.wait_ge(nat_used, t + 1 + CREDIT)
                alone(dve)
                c.step(nc.vector.max(top[:, R8:K], rest[:]))
                c.wait()
                alone(dve)
                c.link(nc.vector.max_index(topi[:, R8:K], top[:, R8:K], rest[:]))
                c.link(nc.vector.tensor_scalar(off[:], top[:], 0.0, SKIP, ALU.is_le, ALU.mult))
                c.link(nc.vector.tensor_tensor(nbr[:, bass.ds(t * K, K)], topi[:], off[:], ALU.add))
                c.link(nc.vector.tensor_scalar(off[:], top[:], 0.0, 2.0 * NEG, ALU.is_gt, ALU.mult))
                c.link(nc.vector.tensor_scalar(cap[:, bass.ds(t * K, K)], off[:], -NEG, None, ALU.add))
                assert c.n == FIND

            def norm(n, b):
                t = n * 2 + b
                c = Chain(dve, dve_norm, t * NORM)
                dve.wait_ge(layer0_mm, t + 1 + CREDIT)
                dve.wait_ge(xb_ready, t + 1)
                nc.vector.tensor_tensor(xn[:, b, :], acc[b][:], xn[:, b, :], ALU.add).then_inc(dve_norm, 1)
                c.n += 1
                c.wait()
                c.step(nc.vector.bn_stats(stats[:], xn[:, b, :]))
                c.wait()
                alone(dve)
                nc.vector.bn_aggr(mv[:], stats[:]).then_inc(var_ready, 1)
                dve.wait_ge(sd_ready, t + 1)
                c.link(nc.vector.reciprocal(rstd[:], sd[:]))
                dve.wait_ge(x1_stored[b], 16 * (n + 1))
                dve.wait_ge(x1T_tr, t + 1)
                nc.vector.tensor_scalar(x1[:, b, :], xn[:, b, :], mv[:, 0:1], rstd[:, 0:1],
                                        ALU.subtract, ALU.mult).then_inc(x1_ready, 1)
                dve.wait_ge(x1_ready, t + 1 + CREDIT)
                assert c.n == NORM

            def rows(n, b):
                t = n * 2 + b
                dve.wait_ge(wh_ready, t + 1 + 1)
                nc.vector.tensor_tensor(prod[:], row[:, b, 0:F].unsqueeze(1).to_broadcast([P, 2, F]), a12[:],
                                        ALU.mult).then_inc(dve_row, 1)
                dve.wait_ge(dve_row, t + 1)
                nc.vector.tensor_reduce(row[:, b, F:ROW], prod[:].rearrange("p a (h k) -> p (a h) k", k=HID),
                                        AX.X, ALU.add).then_inc(row_ready, 1)
                dve.wait_ge(row_ready, t + 1)
                nc.vector.tensor_copy(e_src[:, bass.ds(t * HEADS, HEADS)], row[:, b, F:F + HEADS]).then_inc(src_kept, 1)

            dve.wait_ge(consts_in, 16 * 12)
            find(0, 0)
            norm(0, 0)
            with dve.Fori(0, T // 2 - 1) as n:
                find(n, 1)
                norm(n, 1)
                rows(n, 0)
                find(n + 1, 0)
                norm(n + 1, 0)
                rows(n, 1)
            find(T // 2 - 1, 1)
            norm(T // 2 - 1, 1)
            rows(T // 2 - 1, 0)
            rows(T // 2 - 1, 1)

            def attend(n, b):
                t = n * 2 + b
                c = Chain(dve, dve_att, t * ATT)
                g = gath[b]
                dve.wait_ge(gathered[b], 16 * K * (n + 1))
                dve.wait_ge(e_ready, t + 1)
                own = e_src[:, bass.ds(t * HEADS, HEADS)].unsqueeze(1).to_broadcast([P, K, HEADS])
                c.link(nc.vector.tensor_tensor(z[:], g[:, :, F + HEADS:ROW], own, ALU.add))
                c.link(nc.vector.scalar_tensor_tensor(out=z[:], in0=z[:], scalar=ALPHA, in1=z[:], op0=ALU.mult, op1=ALU.max))
                c.link(nc.vector.tensor_tensor(z[:], z[:], cap[:, bass.ds(t * K, K)].unsqueeze(2).to_broadcast([P, K, HEADS]), ALU.min))
                c.link(nc.vector.tensor_reduce(zmax[:], z[:].rearrange("p k h -> p h k"), AX.X, ALU.max))
                nc.vector.tensor_tensor(z[:], z[:], zmax[:].unsqueeze(1).to_broadcast([P, K, HEADS]),
                                        ALU.subtract).then_inc(z_ready, 1)
                dve.wait_ge(e_ready, t + 2)
                c.link(nc.vector.tensor_reduce(zsum[:], e[:].rearrange("p k h -> p h k"), AX.X, ALU.add))
                c.link(nc.vector.reciprocal(zrec[:], zsum[:]))
                c.link(nc.vector.tensor_tensor(e[:], e[:], zrec[:].unsqueeze(1).to_broadcast([P, K, HEADS]), ALU.mult))
                gk = g[:, :, 0:F].rearrange("p k (h i) -> p k h i", i=HID)
                c.link(nc.vector.tensor_tensor(gk, gk, e[:].unsqueeze(3).to_broadcast([P, K, HEADS, HID]), ALU.mult))
                nc.vector.tensor_tensor(g[:, 0:K // 2, 0:F], g[:, 0:K // 2, 0:F], g[:, K // 2:K, 0:F],
                                        ALU.add).then_inc(weighted, 1)
                assert c.n == ATT

            def elu(t, h):
                dve.wait_ge(hexp_ready, t + 1)
                dve.wait_ge(en_tr, t + 1)
                nc.vector.scalar_tensor_tensor(out=en, in0=h, scalar=0.0, in1=hexp, op0=ALU.max,
                                               op1=ALU.add).then_inc(en_ready, 1)
                dve.wait_ge(en_ready, t + 1 + CREDIT)

            def ln2_sum(g, j):
                if j == 0:
                    dve.wait_ge(x1r_in, 16 * (g + 1))
                dve.wait_ge(y_copied, g * GROUP + j + 1 + CREDIT)
                base = (g * GROUP + j) * 2
                nc.vector.tensor_tensor(y[:, j, :], y[:, j, :], x1r[:, j, :], ALU.add).then_inc(dve_ln2, 1)
                dve.wait_ge(dve_ln2, base + 1)
                nc.vector.bn_stats(stats2[:], y[:, j, :]).then_inc(dve_ln2, 1)
                dve.wait_ge(dve_ln2, base + 2)
                alone(dve)
                nc.vector.bn_aggr(mv2[:, j, :], stats2[:]).then_inc(var2_ready, 1)
                dve.wait_ge(var2_ready, g * GROUP + j + 1)

            def ln2_scale(g):
                dve.wait_ge(sd2_ready, g + 1)
                nc.vector.reciprocal(rstd2[:], sd2[:]).then_inc(dve_en, 1)
                dve.wait_ge(dve_en, g + 1)
                for j in range(GROUP):
                    last = nc.vector.tensor_scalar(y[:, j, :], y[:, j, :], mv2[:, j, 0:1], rstd2[:, j:j + 1],
                                                   ALU.subtract, ALU.mult)
                last.then_inc(y_ready, 1)
                dve.wait_ge(y_ready, g + 1)

            def group(g, first, last):
                for j in range(GROUP):
                    t = g * GROUP + j
                    if not (last and j == GROUP - 1):
                        attend(g * (GROUP // 2) + (j + 1) // 2, (j + 1) % 2)
                    elu(t, acc[j % 2][:])
                    if not first:
                        ln2_sum(g - 1, j)
                if not first:
                    ln2_scale(g - 1)

            nc.vector.tensor_reduce(flagp[:, 0:1], cap[:, K - 1:T * K:K], AX.X, ALU.max).then_inc(flagp_ready, 1)
            nc.vector.tensor_reduce(flagp[:, 1:2], cap[:, 0:T * K:K], AX.X, ALU.min).then_inc(flagp_ready, 1)
            dve.wait_ge(flagp_ready, 2)
            nc.vector.tensor_scalar(flagp[:, 0:1], flagp[:, 0:1], 0.0, None, ALU.is_gt).then_inc(flagp_ready, 1)
            nc.vector.tensor_scalar(flagp[:, 1:2], flagp[:, 1:2], 0.0, None, ALU.is_lt).then_inc(flagp_ready, 1)
            dve.wait_ge(flagp_ready, 4)
            nc.vector.tensor_tensor(flagp[:, 0:1], flagp[:, 0:1], flagp[:, 1:2], ALU.add).then_inc(flagp_ready, 1)

            dve.wait_ge(src_kept, T + CREDIT)
            attend(0, 0)
            group(0, True, False)
            with dve.Fori(1, NG - 1) as g:
                group(g, False, False)
            group(NG - 1, False, True)
            for j in range(GROUP):
                ln2_sum(NG - 1, j)
            ln2_scale(NG - 1)

            dve.wait_ge(flag_mm, 1)
            nc.vector.tensor_copy(flag[:], whp[0:1, 0:1]).then_inc(flag_ready, 1)
            dve.wait_ge(flag_ready, 1)

            def heads(ap):
                return ap.rearrange("p (h i) -> p h i", i=HID)

            def general_step(t, k):
                s = t * STEPS + k
                c = Chain(dve, dve_gen, s * GEN + t * 4 + 3)
                dve.wait_ge(gen_rows_in, 16 * (s + 1))
                c.step(nc.vector.tensor_scalar(gen_cap[:], gen_adj[:, bass.ds(k * K, K)], 0.0, 2.0 * NEG, ALU.is_gt, ALU.mult))
                own = e_src[:, bass.ds(t * HEADS, HEADS)].unsqueeze(1).to_broadcast([P, K, HEADS])
                c.link(nc.vector.tensor_tensor(z[:], gen_g[:, :, F + HEADS:ROW], own, ALU.add))
                c.step(nc.vector.tensor_scalar(gen_cap[:], gen_cap[:], -NEG, None, ALU.add))
                c.link(nc.vector.scalar_tensor_tensor(out=z[:], in0=z[:], scalar=ALPHA, in1=z[:], op0=ALU.mult, op1=ALU.max))
                c.link(nc.vector.tensor_tensor(z[:], z[:], gen_cap[:].unsqueeze(2).to_broadcast([P, K, HEADS]), ALU.min))
                c.link(nc.vector.tensor_reduce(zmax[:], z[:].rearrange("p k h -> p h k"), AX.X, ALU.max))
                c.link(nc.vector.tensor_tensor(zmax[:], zmax[:], gen_m[:], ALU.max))
                c.step(nc.vector.tensor_tensor(gen_fade[:], gen_m[:], zmax[:], ALU.subtract))
                nc.vector.tensor_tensor(z[:], z[:], zmax[:].unsqueeze(1).to_broadcast([P, K, HEADS]),
                                        ALU.subtract).then_inc(gen_z, 1)
                c.wait()
                c.link(nc.vector.tensor_copy(gen_m[:], zmax[:]))
                dve.wait_ge(gen_e, 2 * (s + 1))
                c.step(nc.vector.tensor_reduce(gen_part[:, 0:HEADS], e[:].rearrange("p k h -> p h k"), AX.X, ALU.add))
                c.link(nc.vector.tensor_tensor(zsum[:], zsum[:], gen_scale[:], ALU.mult))
                c.link(nc.vector.tensor_tensor(zsum[:], zsum[:], gen_part[:, 0:HEADS], ALU.add))
                gk = gen_g[:, :, 0:F].rearrange("p k (h i) -> p k h i", i=HID)
                c.link(nc.vector.tensor_tensor(gk, gk, e[:].unsqueeze(3).to_broadcast([P, K, HEADS, HID]), ALU.mult))
                c.step(nc.vector.tensor_tensor(heads(gen_h), heads(gen_h), gen_scale[:].unsqueeze(2).to_broadcast([P, HEADS, HID]),
                                               ALU.mult))
                c.link(nc.vector.tensor_reduce(gen_part, gen_g[:, :, 0:F].rearrange("p k f -> p f k"), AX.X, ALU.add))
                c.link(nc.vector.tensor_tensor(gen_h, gen_h, gen_part, ALU.add))
                nc.vector.memset(zrec[:], 0.0).then_inc(gen_rows_used, 1)
                assert c.n == GEN, c.n

            with dve.If(dve.value_load(flag[0:1, 0:1]) > 0):
                with dve.Fori(NG, 2 * NG) as g:
                    with dve.Fori(0, GROUP) as j:
                        t = (g - NG) * GROUP + j
                        c = Chain(dve, dve_gen, t * (STEPS * GEN + 4))
                        c.step(nc.vector.memset(gen_m[:], LOWEST))
                        c.step(nc.vector.memset(zsum[:], 0.0))
                        c.link(nc.vector.memset(gen_h, 0.0))
                        dve.wait_ge(gen_adj_in, 16 * (t + 1))
                        alone(dve)
                        with dve.Fori(0, STEPS) as k:
                            general_step(t, k)
                        dve.wait_ge(dve_gen, t * (STEPS * GEN + 4) + 3 + STEPS * GEN)
                        nc.vector.reciprocal(zrec[:], zsum[:]).then_inc(dve_gen, 1)
                        dve.wait_ge(dve_gen, t * (STEPS * GEN + 4) + 4 + STEPS * GEN)
                        nc.vector.tensor_tensor(heads(gen_h), heads(gen_h), zrec[:].unsqueeze(2).to_broadcast([P, HEADS, HID]),
                                                ALU.mult).then_inc(gen_h_ready, 1)
                        dve.wait_ge(gen_h_ready, t + 1)
                        elu(t + T, gen_h)
                    for j in range(GROUP):
                        ln2_sum(g, j)
                    ln2_scale(g)

        @block.scalar
        def _(act):
            act.sem_inc(support_act, 1)
            act.sem_inc(x1T_ready, 1)
            act.sem_inc(wh_ready, 1)
            act.sem_inc(e_ready, 1)
            act.sem_inc(encT_ready, 1)
            act.sem_inc(y_copied, CREDIT)
            with act.Fori(0, T // 2) as n:
                act.wait_ge(support_mm, n * 2 + 1 + CREDIT)
                nc.scalar.activation(support[:, n * 2, :], acc[0][:], ACT.Copy).then_inc(support_act, 1)

            def root(t):
                act.wait_ge(var_ready, t + 1)
                nc.scalar.activation(sd[:], mv[:, 1:2], ACT.Sqrt, bias=eps[:]).then_inc(sd_ready, 1)

            def x1T_out(t):
                act.wait_ge(x1T_tr, t + 1 + CREDIT)
                act.wait_ge(wh_mm, t + 1)
                nc.scalar.activation(x1T[:].rearrange("p c i -> p (c i)"), trp[:], ACT.Copy).then_inc(x1T_ready, 1)

            def wh_out(n, b):
                t = n * 2 + b
                act.wait_ge(wh_mm, t + 2)
                act.wait_ge(src_kept, t + 1)
                act.wait_ge(row_stored[b], 16 * (n + 1))
                nc.scalar.activation(row[:, b, 0:F], whp[:], ACT.Copy).then_inc(wh_ready, 1)

            act.wait_ge(consts_set, 4)
            root(0)
            with act.Fori(0, T // 2 - 1) as n:
                for b in range(2):
                    x1T_out(n * 2 + b)
                    root(n * 2 + b + 1)
                    wh_out(n, b)
            x1T_out(T - 2)
            root(T - 1)
            wh_out(T // 2 - 1, 0)
            x1T_out(T - 1)
            wh_out(T // 2 - 1, 1)

            def score_exp(t):
                act.wait_ge(z_ready, t + 1)
                nc.scalar.activation(e[:], z[:], ACT.Exp).then_inc(e_ready, 1)

            def elu_exp(t, h):
                act.wait_ge(en_ready, t + CREDIT)
                nc.scalar.activation(hneg, h, ACT.Relu, scale=-1.0).then_inc(hneg_ready, 1)
                act.wait_ge(hneg_ready, t + 1)
                nc.scalar.activation(hexp, hneg, ACT.Exp, scale=-1.0).then_inc(hexp_ready, 1)

            def enc_out(t, j):
                act.wait_ge(en_tr, t + 2)
                nc.scalar.activation(encT[:, :, j * P:(j + 1) * P], trp[:].rearrange("p (c i) -> p c i", i=P),
                                     ACT.Identity, bias=minus1[:]).then_inc(encT_ready, 1)

            def hidden(g, n, dst, src, bias):
                act.wait_ge(mlp_mm, g * 5 + n + 1)
                nc.scalar.activation(dst, src, ACT.Relu, bias=bias).then_inc(mlp_act, 1)

            def group(g, first, last):
                for j in range(GROUP):
                    t = g * GROUP + j
                    if not (last and j == GROUP - 1):
                        score_exp(t + 1)
                    act.wait_ge(sum_mm, t + 1 + CREDIT)
                    elu_exp(t, acc[j % 2][:])
                    enc_out(t, j)
                if not first:
                    roots2(g - 1)
                mlp_out(g, first)

            def mlp_out(g, first):
                for m in range(M1 // P):
                    hidden(g, m, h1[:, m, :], mlp[m][:], b1[:, m:m + 1])
                hidden(g, 2, h2, mlp[0][:], b2[:, 0:1])
                for m in range(M3 // P):
                    hidden(g, 3 + m, h3[:, m, :], mlp[(m + 1) % 2][:], b3[:, m:m + 1])
                if not first:
                    act.wait_ge(out_stored, 16 * g)
                for j in range(GROUP):
                    act.wait_ge(out_mm, g * GROUP + j + 1 + CREDIT)
                    nc.scalar.activation(y[:, j, :], outp[j % 2][:], ACT.Copy).then_inc(y_copied, 1)

            def roots2(g):
                act.wait_ge(var2_ready, (g + 1) * GROUP)
                nc.scalar.activation(sd2[:], mv2[:, :, 1], ACT.Sqrt, bias=eps[:]).then_inc(sd2_ready, 1)

            score_exp(0)
            group(0, True, False)
            with act.Fori(1, NG - 1) as g:
                group(g, False, False)
            group(NG - 1, False, True)
            roots2(NG - 1)

            act.wait_ge(flag_ready, 1)
            with act.If(act.value_load(flag[0:1, 0:1]) > 0):
                with act.Fori(NG, 2 * NG) as g:
                    for j in range(GROUP):
                        t = (g - NG) * GROUP + j
                        with act.Fori(0, STEPS) as k:
                            s = t * STEPS + k
                            act.wait_ge(gen_z, s + 1)
                            nc.scalar.activation(e[:], z[:], ACT.Exp).then_inc(gen_e, 1)
                            nc.scalar.activation(gen_scale[:], gen_fade[:], ACT.Exp).then_inc(gen_e, 1)
                        act.wait_ge(gen_h_ready, t + 1)
                        elu_exp(t + T, gen_h)
                        enc_out(t + T, j)
                    mlp_out(g, False)
                    roots2(g)

        @block.gpsimd
        def _(pool):
            nc.gpsimd.memset(ident[:], 0.0).then_inc(ident_zero, 1)
            pool.wait_ge(ident_zero, 1)
            nc.gpsimd.affine_select(out=ident[:], in_=ident[:], compare_op=ALU.not_equal, fill=1.0, base=0,
                                    pattern=[[-1, P]], channel_multiplier=1).then_inc(ident_zero, 1)
            pool.wait_ge(consts_in, 16 * 12)

            def add_bias(n, b):
                pool.wait_ge(xn_in[b], 16 * (n + 1))
                nc.gpsimd.tensor_tensor(xn[:, b, :], xn[:, b, :], bias0[:], ALU.add).then_inc(xb_ready, 1)

            with pool.Fori(0, T // 2) as n:
                for b in range(2):
                    add_bias(n, b)

            for b in range(2):
                pool.wait_ge(row_stored[b], 16 * (T // 2 + 1))
            with pool.Fori(0, T // 2) as n:
                for b in range(2):
                    t = n * 2 + b
                    pool.wait_ge(sum_mm, t + 1)
                    nc.gpsimd.tensor_copy(idx[:, b, :], nbr[:, bass.ds(t * K, K)]).then_inc(idx_ready, 1)
                    pool.wait_ge(idx_ready, t + 1)
                    alone(pool)
                    for k in range(K):
                        pool.indirect_dma_start(gath[b][:, k, :], None, d["table"],
                                                bass.IndirectOffsetOnAxis(ap=idx[:, b, k:k + 1], axis=0),
                                                bounds_check=N - 1, oob_is_err=False).then_inc(gathered[b], 16)

        @block.tensor
        def _(pe):
            pe.sem_inc(support_mm, CREDIT)
            pe.sem_inc(layer0_mm, CREDIT)
            pe.sem_inc(x1T_tr, CREDIT)
            pe.sem_inc(wh_mm, 1)
            pe.sem_inc(sum_mm, CREDIT)
            pe.sem_inc(en_tr, 1)
            pe.sem_inc(out_mm, CREDIT)
            pe.wait_ge(consts_in, 16 * 12)
            pe.wait_ge(ident_zero, 2)
            pe.wait_ge(consts_set, 4)
            with pe.Fori(0, T // 2) as n:
                for b, copied in ((0, support_act), (1, support_dve)):
                    t = n * 2 + b
                    pe.wait_ge(xT_in[b], 16 * (n + 1))
                    pe.wait_ge(copied, n + 1)
                    for c in range(FC):
                        last = nc.tensor.matmul(acc[b][:], xT[:, b, c, :], w0[:, c, :], start=(c == 0), stop=(c == FC - 1))
                    last.then_inc(support_mm, 1)

            def layer0(n, b, chunks):
                t = n * 2 + b
                for c in chunks:
                    if c == 0:
                        pe.wait_ge(strip_in[b], 16 * (n + 1))
                        pe.wait_ge(x1_ready, t + 1)
                    last = nc.tensor.matmul(acc[b][:], strip[b][:, c, :], support[:, c, :], start=(c == 0), stop=(c == T - 1))
                    if c == T - 1:
                        last.then_inc(layer0_mm, 1)

            def turn(t, b):
                pe.wait_ge(x1_ready, t + 1 + CREDIT)
                pe.wait_ge(x1T_ready, t + 1)
                for c in range(FC):
                    last = nc.tensor.transpose(trp[:, c * P:(c + 1) * P], x1[:, b, c * P:(c + 1) * P], ident[:])
                last.then_inc(x1T_tr, 1)

            def wh(t):
                pe.wait_ge(x1T_ready, t + 2)
                pe.wait_ge(wh_ready, t + 1)
                for c in range(FC):
                    last = nc.tensor.matmul(whp[:], x1T[:, c, :], wcat[:, c, :], start=(c == 0), stop=(c == FC - 1))
                last.then_inc(wh_mm, 1)

            pe.wait_ge(support_act, T // 2 + 1)
            pe.wait_ge(support_dve, T // 2 + 1)
            HALF = T // 2
            layer0(0, 0, range(T))
            with pe.Fori(0, T // 2 - 1) as n:
                for b in range(2):
                    layer0(n + b, 1 - b, range(HALF))
                    turn(n * 2 + b, b)
                    layer0(n + b, 1 - b, range(HALF, T))
                    wh(n * 2 + b)
            layer0(T // 2 - 1, 1, range(HALF))
            turn(T - 2, 0)
            layer0(T // 2 - 1, 1, range(HALF, T))
            wh(T - 2)
            turn(T - 1, 1)
            wh(T - 1)

            def neighbour_sum(t, b):
                pe.wait_ge(weighted, t + 1)
                pe.wait_ge(en_ready, t + 1)
                for k in range(K // 2):
                    last = nc.tensor.matmul(acc[b][:], ident[:], gath[b][:, k, 0:F], start=(k == 0), stop=(k == K // 2 - 1))
                last.then_inc(sum_mm, 1)

            def turn_en(t):
                pe.wait_ge(en_ready, t + 1 + CREDIT)
                pe.wait_ge(encT_ready, t + 1)
                for c in range(FC):
                    last = nc.tensor.transpose(trp[:, c * P:(c + 1) * P], en[:, c * P:(c + 1) * P], ident[:])
                last.then_inc(en_tr, 1)

            def dense(dst, w, src, m):
                n = w.shape[1]
                for c in range(n):
                    last = nc.tensor.matmul(dst[:], w[:, c, m * P:(m + 1) * P], src[:, c, :], start=(c == 0), stop=(c == n - 1))
                last.then_inc(mlp_mm, 1)

            def mlps(g):
                pe.wait_ge(encT_ready, (g + 1) * GROUP + 1)
                for m in range(M1 // P):
                    dense(mlp[m], w1, encT, m)
                pe.wait_ge(mlp_act, g * 5 + 2)
                dense(mlp[0], w2, h1, 0)
                pe.wait_ge(mlp_act, g * 5 + 3)
                for m in range(M3 // P):
                    dense(mlp[(m + 1) % 2], w3, h2.unsqueeze(1), m)
                pe.wait_ge(mlp_act, g * 5 + 5)
                for j in range(GROUP):
                    t = g * GROUP + j
                    pe.wait_ge(y_copied, t + 1)
                    nc.tensor.matmul(outp[j % 2][:], ones[:], b4[:], start=True, stop=False)
                    for c in range(M3 // P):
                        last = nc.tensor.matmul(outp[j % 2][:], h3[:, c, j * P:(j + 1) * P], w4[:, c, :],
                                                start=False, stop=(c == M3 // P - 1))
                    last.then_inc(out_mm, 1)

            def group(g, last):
                for j in range(GROUP):
                    t = g * GROUP + j
                    if not (last and j == GROUP - 1):
                        neighbour_sum(t + 1, (j + 1) % 2)
                    turn_en(t)
                mlps(g)

            pe.wait_ge(flagp_ready, 5)
            pe.wait_ge(wh_ready, T + 1)
            nc.tensor.matmul(whp[0:1, 0:1], flagp[:, 0:1], onesc[:], start=True, stop=True).then_inc(flag_mm, 1)
            neighbour_sum(0, 0)
            group(0, False)
            with pe.Fori(1, NG - 1) as g:
                group(g, False)
            group(NG - 1, True)

            pe.wait_ge(flag_ready, 1)
            with pe.If(pe.value_load(flag[0:1, 0:1]) > 0):
                with pe.Fori(NG, 2 * NG) as g:
                    for j in range(GROUP):
                        turn_en(g * GROUP + j)
                    mlps(g)


def kernel(**inputs):
    import concourse.bacc as bacc
    from concourse.bass_utils import run_bass_kernel_spmd

    a = {k: np.ascontiguousarray(v) for k, v in inputs.items()}

    def chunks(w):
        return np.ascontiguousarray(w.reshape(-1, P, w.shape[1]).transpose(1, 0, 2))

    def column(v):
        return np.ascontiguousarray(v.reshape(-1, P).T)

    arrays = {
        "x": a["x"],
        "adj": a["adj"],
        "xT": np.ascontiguousarray(a["x"].reshape(T, P, FC, P).transpose(0, 3, 2, 1)),
        "adjT": np.ascontiguousarray(a["adj"].reshape(T, P, T, P).transpose(0, 3, 2, 1)),
        "w0": chunks(a["L0_gnn_weight"]),
        "wcat": chunks(a["L1_gnn_W"].transpose(1, 0, 2).reshape(F, HEADS * HID)),
        "w1": chunks(a["L1_gnn_W1"].T),
        "w2": chunks(a["L1_gnn_W2"].T),
        "w3": chunks(a["L1_gnn_W3"].T),
        "w4": chunks(a["L1_gnn_W4"].T),
        "b1": column(a["L1_gnn_b1"]),
        "b2": column(a["L1_gnn_b2"]),
        "b3": column(a["L1_gnn_b3"]),
        "b4": a["L1_gnn_b4"].reshape(1, F),
        "bias0": a["L0_gnn_bias"].reshape(1, F),
        "a12": np.concatenate([a["L1_gnn_a1"].reshape(1, F), a["L1_gnn_a2"].reshape(1, F)], axis=1),
    }
    nc = bacc.Bacc("TRN2", target_bir_lowering=False, num_devices=1)
    d = {k: nc.dram_tensor(f"{k}_dram", v.shape, F32, kind="ExternalInput").ap() for k, v in arrays.items()}
    d["out"] = nc.dram_tensor("out_dram", (N, F), F32, kind="ExternalOutput").ap()
    d["x1"] = nc.dram_tensor("x1_dram", (N, F), F32, kind="Internal").ap()
    d["table"] = nc.dram_tensor("table_dram", (N, ROW), F32, kind="Internal").ap()
    build(nc, d)
    r = run_bass_kernel_spmd(nc, [{f"{k}_dram": v for k, v in arrays.items()}], core_ids=[0])
    return r.results[0]["out_dram"]
```
